# Optimizing a Trainium2 kernel written in Bass

```python
import numpy as np
import jax
import jax.numpy as jnp

def _softmax(x, axis=-1):
    return jax.nn.softmax(x, axis=axis)

def _gelu(x):
    return jax.nn.gelu(x, approximate=True)

def _silu(x):
    return jax.nn.silu(x)

def _sigmoid(x):
    return jax.nn.sigmoid(x)

def _layernorm(x, axis=-1, eps=1e-05):
    m = jnp.mean(x, axis=axis, keepdims=True)
    v = jnp.var(x, axis=axis, keepdims=True)
    return (x - m) / jnp.sqrt(v + eps)

def _scatter_add(tgt, idx, src, axis=0):
    return tgt.at[idx].add(src)

def _segment_sum(src, seg, n):
    return jax.ops.segment_sum(src, seg, n)
kernel_name = 'mk_rec_standalone_d1_rec_r8_f6c60e'

def setup_inputs(seed: int=0):
    np.random.seed(seed)
    _w = jnp.asarray

    def _rec_inputs():
        import jax
        import jax.numpy as jnp
        _rk = jax.random.key(seed)
        r_x = -0.000520686 + 1.00062 * jax.random.normal(jax.random.fold_in(_rk, 1), (512, 32, 32), jnp.float32)
        return r_x
    r_x = _rec_inputs()

    def _L0_rec_setup():
        import jax, jax.numpy as jnp
        import numpy as np

        def _cin(x, Ws, bs):
            B, F, D = x.shape
            h = x
            directs = []
            n_layers = len(Ws)
            for i, (W, b) in enumerate(zip(Ws, bs)):
                O = W.shape[0]
                H = h.shape[1]
                z = jnp.einsum('bhd,bmd,ohm->bod', h, x, W.reshape(O, H, F))
                z = jax.nn.relu(z + b[None, :, None])
                if i < n_layers - 1:
                    half = O // 2
                    h, direct = (z[:, :half, :], z[:, half:, :])
                else:
                    direct = z
                directs.append(direct)
            out = jnp.concatenate(directs, axis=1)
            return jnp.sum(out, axis=-1)
        key = jax.random.key(seed)
        ks = jax.random.split(key, 4)
        B, F, D = (256, 32, 32)
        x = jax.random.normal(ks[0], (B, F, D), dtype=jnp.float32)
        W0 = jax.random.normal(ks[1], (128, 32 * F), dtype=jnp.float32) * 0.05
        W1 = jax.random.normal(ks[2], (128, 64 * F), dtype=jnp.float32) * 0.05
        W2 = jax.random.normal(ks[3], (1, 64 * F), dtype=jnp.float32) * 0.05
        return {'x': x, 'W0': W0, 'b0': jnp.zeros((128,), jnp.float32), 'W1': W1, 'b1': jnp.zeros((128,), jnp.float32), 'W2': W2, 'b2': jnp.zeros((1,), jnp.float32)}
    _L0_rec_all = _L0_rec_setup()
    _L0_rec_in = {k: v for k, v in _L0_rec_all.items() if k in ('W0', 'b0', 'W1', 'b1', 'W2', 'b2')}
    del _L0_rec_all
    return {'r_x': r_x, 'L0_rec_W0': _L0_rec_in['W0'], 'L0_rec_b0': _L0_rec_in['b0'], 'L0_rec_W1': _L0_rec_in['W1'], 'L0_rec_b1': _L0_rec_in['b1'], 'L0_rec_W2': _L0_rec_in['W2'], 'L0_rec_b2': _L0_rec_in['b2']}

def reference(r_x, L0_rec_W0, L0_rec_b0, L0_rec_W1, L0_rec_b1, L0_rec_W2, L0_rec_b2):
    import jax
    import jax.numpy as jnp

    def _L0_rec_ref(x, W0, b0, W1, b1, W2, b2):
        import jax, jax.numpy as jnp
        import numpy as np

        def _cin(x, Ws, bs):
            B, F, D = x.shape
            h = x
            directs = []
            n_layers = len(Ws)
            for i, (W, b) in enumerate(zip(Ws, bs)):
                O = W.shape[0]
                H = h.shape[1]
                z = jnp.einsum('bhd,bmd,ohm->bod', h, x, W.reshape(O, H, F))
                z = jax.nn.relu(z + b[None, :, None])
                if i < n_layers - 1:
                    half = O // 2
                    h, direct = (z[:, :half, :], z[:, half:, :])
                else:
                    direct = z
                directs.append(direct)
            out = jnp.concatenate(directs, axis=1)
            return jnp.sum(out, axis=-1)
        return _cin(x, (W0, W1, W2), (b0, b1, b2))
    y = _L0_rec_ref(r_x, L0_rec_W0, L0_rec_b0, L0_rec_W1, L0_rec_b1, L0_rec_W2, L0_rec_b2)
    return y

_drawn_inputs = setup_inputs


def setup_inputs(seed=0):
    import zlib

    import numpy as np

    out = dict(_drawn_inputs(seed))
    spreads = {'L0_rec_b0': (0.0, 0.1), 'L0_rec_b1': (0.0, 0.1)}
    factors = {}
    for name, (base, spread) in spreads.items():
        noise = np.random.default_rng([zlib.crc32(name.encode()), seed]).standard_normal(out[name].shape)
        drawn = base * np.exp(spread * noise) if base else spread * noise
        out[name] = jnp.asarray(drawn.astype(out[name].dtype))
    for name, factor in factors.items():
        out[name] = (out[name] * factor).astype(out[name].dtype)
    return out
```

```python
from contextlib import ExitStack

import concourse.bass as bass
from concourse import mybir

F32 = mybir.dt.float32
F32R = mybir.dt.float32r
BF16 = mybir.dt.bfloat16
ALU = mybir.AluOpType
ACT = mybir.ActivationFunctionType
AX_X = mybir.AxisListType.X

P = 128
FIELDS = 32
D = 32
CHUNK = 512
PAIR = 2 * CHUNK
HALF = 64
T0 = 5
T1 = 16
SLOTS = T0 + T1
SYM_ROWS = 16 * FIELDS + FIELDS // 2
PARTS = 3
RING = 7
XE_RING = 3
AHEAD = 4
LO_ON_VECTOR = (2, 6, 8, 10, 12, 14, 16, 18)
LO_LAG = 2
B_PAIR = PAIR // D
Z2_COLS = PAIR // P


def count_lo(k, on_vector, first=0):
    return sum((s in LO_ON_VECTOR) == on_vector for s in range(first, k + 1))


class Slot:

    def __init__(self, i, k, last=False):
        first = T0 if last else 0
        self.k, self.i = k, i
        self.layer1 = k >= T0
        self.pair = i if self.layer1 else i + 1
        self.tile = k - T0 if self.layer1 else k
        self.before = T0 + SLOTS * i + (k - first)
        self.done = self.before + 1
        place = T0 + k - first if not last else T0 + SLOTS * i + k - first
        self.ring = place % RING
        self.xe = [(2 * place + c) % XE_RING for c in range(2)]
        self.on_vector = k in LO_ON_VECTOR
        self.lo = (count_lo(T0 - 1, self.on_vector) + count_lo(SLOTS - 1, self.on_vector) * i
                   + count_lo(k, self.on_vector, first))


class FirstSlot(Slot):

    def __init__(self, k):
        self.k, self.layer1, self.pair, self.tile = k, False, 0, k
        self.before, self.done = k, k + 1
        self.ring = k % RING
        self.xe = [(2 * k + c) % XE_RING for c in range(2)]
        self.on_vector = k in LO_ON_VECTOR
        self.lo = count_lo(k, self.on_vector)


def cin_kernel(nc, x, w0_straight, w0_mirrored, b0, w1, b1, w2, b2, sel, ident, pick_chunk, pick_b, out):
    n_cols = x.shape[1]
    pairs = n_cols // PAIR
    last = pairs - 1
    q_cols = n_cols // 4
    early = PAIR
    samples = n_cols // D

    with ExitStack() as ctx:
        def sb(name, shape, dt=F32):
            return ctx.enter_context(nc.sbuf_tensor(name, shape, dt))

        def psum(name, shape):
            return ctx.enter_context(nc.psum_tensor(name, shape, F32))

        def sem(name):
            return ctx.enter_context(nc.semaphore(name))

        w0a = sb("w0a", [P, T0, P])
        w0b = sb("w0b", [P, T0, P])
        w1s = sb("w1s", [P, T1, P])
        w0_hi = sb("w0_hi", [P, T0, P], F32R)
        w0_lo = sb("w0_lo", [P, T0, P], F32R)
        w1_hi = sb("w1_hi", [P, T1, P], F32R)
        w1_lo = sb("w1_lo", [P, T1, P], F32R)
        w2s = sb("w2s", [HALF, FIELDS])
        b0s = sb("b0s", [P, 1])
        b1s = sb("b1s", [P, 1])
        b2s = sb("b2s", [P, 1])
        sels = sb("sels", [PARTS * FIELDS, SLOTS, P], BF16)
        idents = sb("idents", [P, P])
        pick_chunks = sb("pick_chunks", [HALF, 2])
        pick_bs = sb("pick_bs", [P, 4])
        xq = sb("xq", [P, q_cols])
        xq_parts = sb("xq_parts", [P, PARTS, q_cols], BF16)
        xp0 = sb("xp0", [PARTS * FIELDS, PAIR], BF16)
        xp1 = sb("xp1", [PARTS * FIELDS, PAIR], BF16)
        x4 = sb("x4", [P, PAIR])
        xv = sb("xv", [HALF, CHUNK])
        prod = sb("prod", [P, RING, PAIR])
        hi = sb("hi", [P, RING, PAIR], F32R)
        lo = sb("lo", [P, RING, PAIR], F32R)
        h1 = sb("h1", [P, PAIR])
        h2 = sb("h2", [HALF, PAIR])
        direct = sb("direct", [P, PAIR])
        sums = sb("sums", [P, samples + B_PAIR])
        v = sb("v", [HALF, CHUNK])
        z2 = sb("z2", [P, Z2_COLS * pairs])
        res = sb("res", [P, 4, P + 1])
        xe = psum("xe", [P, XE_RING, CHUNK])
        acc0 = psum("acc0", [P, 2, CHUNK])
        acc1 = psum("acc1", [P, 2, CHUNK])
        uz = psum("uz", [P, CHUNK])

        parts_dram = nc.dram_tensor("parts_scratch", (PARTS, FIELDS, n_cols), BF16, kind="Internal").ap()

        w0_zeroed = sem("w0_zeroed")
        w0_loaded = sem("w0_loaded")
        w1_loaded = sem("w1_loaded")
        small_loaded = sem("small_loaded")
        final_loaded = sem("final_loaded")
        w0_summed = sem("w0_summed")
        w_hi_ready = sem("w_hi_ready")
        w_lo_ready = sem("w_lo_ready")
        xq_loaded = sem("xq_loaded")
        xq_late_loaded = sem("xq_late_loaded")
        part_ready = sem("part_ready")
        rest_ready = sem("rest_ready")
        early_stored = sem("early_stored")
        late_stored = sem("late_stored")
        xp0_loaded = sem("xp0_loaded")
        xp1_loaded = sem("xp1_loaded")
        x4_loaded = sem("x4_loaded")
        xv_loaded = sem("xv_loaded")
        xe_ready = sem("xe_ready")
        prod_ready = sem("prod_ready")
        hi_ready = sem("hi_ready")
        lo_vector_ready = sem("lo_vector_ready")
        lo_pool_ready = sem("lo_pool_ready")
        slot_done = sem("slot_done")
        h1_ready = sem("h1_ready")
        direct0_ready = sem("direct0_ready")
        direct1_ready = sem("direct1_ready")
        h2_ready = sem("h2_ready")
        direct_summed = sem("direct_summed")
        u_ready = sem("u_ready")
        v_ready = sem("v_ready")
        z2_summed = sem("z2_summed")
        z2_ready = sem("z2_ready")
        turned = sem("turned")
        z2_final = sem("z2_final")
        res_ready = sem("res_ready")
        stored = sem("stored")

        block = ctx.enter_context(nc.Block())

        x_q = x.rearrange("m (q j i) -> j m q i", j=4, i=PAIR // 4)
        parts_q = parts_dram.rearrange("r m (q j i) -> r j m q i", j=4, i=PAIR // 4)
        parts_all = parts_dram.rearrange("r m n -> (r m) n")

        def wait_parts(eng, step, late):
            eng.wait_ge(part_ready, step + PARTS * late)

        @block.sync
        def _(sp):
            early_q = early // (PAIR // 4)
            for j in range(4):
                rows = slice(j * FIELDS, (j + 1) * FIELDS)
                sp.dma_start(xq[rows, 0:early].rearrange("p (q i) -> p q i", i=PAIR // 4),
                             x_q[j][:, 0:early_q, :]).then_inc(xq_loaded, 16)

            def wait_layer0(q):
                halves = 2 * T0 if isinstance(q, int) else 2 * (T0 + SLOTS * (q - 2) + T0)
                sp.wait_ge(xe_ready, halves)
                sp.wait_ge(prod_ready, halves)

            def load_x4(q):
                for j in range(4):
                    sp.dma_start(x4[j * FIELDS:(j + 1) * FIELDS, :], x[:, bass.ds(q * PAIR, PAIR)]).then_inc(x4_loaded, 16)

            def load_xv(q):
                if not isinstance(q, int) or q > 0:
                    sp.wait_ge(v_ready, q)
                for c in range(2):
                    sp.dma_start(xv[c * FIELDS:(c + 1) * FIELDS, :],
                                 x[:, bass.ds(q * PAIR + c * CHUNK, CHUNK)]).then_inc(xv_loaded, 16)

            def load_xp0(q):
                sp.dma_start(xp0[:, :], parts_all[:, bass.ds(q * PAIR, PAIR)]).then_inc(xp0_loaded, 16)

            def load_xp1(q):
                if not isinstance(q, int) or q > 0:
                    sp.wait_ge(xe_ready, 2 * (T0 + SLOTS * q))
                sp.dma_start(xp1[:, :], parts_all[:, bass.ds(q * PAIR, PAIR)]).then_inc(xp1_loaded, 16)

            sp.dma_start(sels[:, :, :], sel).then_inc(small_loaded, 16)
            sp.wait_ge(w0_zeroed, 3)
            whole = 4 * P
            sp.dma_start(w0a[:, 0:4, :], w0_straight[0:whole, :].rearrange("(t p) o -> p t o", p=P)).then_inc(w0_loaded, 16)
            sp.dma_start(w0a[0:SYM_ROWS - whole, 4, :], w0_straight[whole:SYM_ROWS, :]).then_inc(w0_loaded, 16)
            edge = P - FIELDS
            sp.dma_start(w0b[FIELDS:P, 0, :], w0_mirrored[0:edge, :]).then_inc(w0_loaded, 16)
            sp.dma_start(w0b[:, 1:4, :], w0_mirrored[edge:edge + 3 * P, :].rearrange("(t p) o -> p t o", p=P)).then_inc(w0_loaded, 16)
            sp.dma_start(w0b[0:SYM_ROWS - whole, 4, :], w0_mirrored[edge + 3 * P:, :]).then_inc(w0_loaded, 16)
            load_x4(0)
            sp.dma_start(w1s[:, :, :], w1).then_inc(w1_loaded, 16)
            sp.dma_start(b0s[:, :], b0).then_inc(small_loaded, 16)
            sp.dma_start(b1s[:, :], b1).then_inc(small_loaded, 16)
            sp.dma_start(w2s[:, :], w2.rearrange("a (h m) -> (a h) m", m=FIELDS)).then_inc(small_loaded, 16)
            sp.dma_start(b2s[:, :], b2).then_inc(small_loaded, 16)
            sp.dma_start(pick_chunks[:, :], pick_chunk).then_inc(small_loaded, 16)
            load_xv(0)

            def store_parts(r, lo_q, hi_q, done):
                for j in range(4):
                    rows = slice(j * FIELDS, (j + 1) * FIELDS)
                    cols = slice(lo_q * (PAIR // 4), hi_q * (PAIR // 4))
                    sp.dma_start(parts_q[r, j][:, lo_q:hi_q, :],
                                 xq_parts[rows, r, cols].rearrange("p (q i) -> p q i", i=PAIR // 4)).then_inc(done, 16)

            for r in range(PARTS):
                wait_parts(sp, r + 1, 0)
                store_parts(r, 0, early_q, early_stored)
            for j in range(4):
                rows = slice(j * FIELDS, (j + 1) * FIELDS)
                sp.dma_start(xq[rows, early:].rearrange("p (q i) -> p q i", i=PAIR // 4),
                             x_q[j][:, early_q:, :]).then_inc(xq_late_loaded, 16)
            sp.dma_start(idents[:, :], ident).then_inc(final_loaded, 16)
            sp.dma_start(pick_bs[:, :], pick_b).then_inc(final_loaded, 16)
            sp.wait_ge(early_stored, 16 * 4 * PARTS)
            load_xp0(0)
            load_xp1(0)
            wait_layer0(1)
            load_xp0(1)
            load_x4(1)
            for r in range(PARTS):
                wait_parts(sp, r + 1, 1)
                store_parts(r, early_q, q_cols // (PAIR // 4), late_stored)
            load_xp1(1)
            sp.wait_ge(late_stored, 16 * 4 * PARTS)
            with sp.Fori(2, pairs) as q:
                wait_layer0(q)
                load_xp0(q)
                load_x4(q)
                load_xv(q - 1)
                load_xp1(q)
            load_xv(last)
            sp.wait_ge(res_ready, 9)
            sp.dma_start(out.rearrange("(q r) c -> q r c", r=4), res[:, :, :]).then_inc(stored, 16)
            sp.wait_ge(stored, 16)

        @block.tensor
        def _(pe):
            def spread(slot, c):
                if c == 0 and slot.tile == 0:
                    pe.wait_ge(xp1_loaded if slot.layer1 else xp0_loaded, 16 * (slot.pair + 1))
                n = 2 * slot.before + c
                if not isinstance(n, int) or n >= XE_RING:
                    pe.wait_ge(prod_ready, n - XE_RING + 1)
                xp = xp1 if slot.layer1 else xp0
                pe.matmul(xe[:, slot.xe[c], :], sels[:, slot.k, :], xp[:, c * CHUNK:(c + 1) * CHUNK],
                          start=True, stop=True).then_inc(xe_ready, 1)

            def contract(slot, c):
                acc = acc1 if slot.layer1 else acc0
                w_hi, w_lo, tiles = (w1_hi, w1_lo, T1) if slot.layer1 else (w0_hi, w0_lo, T0)
                cols = slice(c * CHUNK, (c + 1) * CHUNK)
                if c == 0:
                    pe.wait_ge(hi_ready, slot.done)
                first, final = slot.tile == 0, slot.tile == tiles - 1
                pe.matmul(acc[:, c, :], w_hi[:, slot.tile, :], hi[:, slot.ring, cols], start=first, stop=False)
                pe.matmul(acc[:, c, :], w_lo[:, slot.tile, :], hi[:, slot.ring, cols], start=False, stop=False)
                if c == 0:
                    pe.wait_ge(lo_vector_ready if slot.on_vector else lo_pool_ready, slot.lo)
                mm = pe.matmul(acc[:, c, :], w_hi[:, slot.tile, :], lo[:, slot.ring, cols], start=False, stop=final)
                if c == 1:
                    mm.then_inc(slot_done, 1)

            def wait_layer2_u(i):
                pe.wait_ge(h2_ready, i + 1)

            def layer2_u(i):
                for c in range(2):
                    mm = pe.matmul(uz[c * FIELDS:(c + 1) * FIELDS, :], w2s[:, :], h2[:, c * CHUNK:(c + 1) * CHUNK],
                                   start=True, stop=True)
                mm.then_inc(u_ready, 1)

            def layer2_z(i):
                pe.wait_ge(v_ready, i + 1)
                for a in range(CHUNK // P):
                    mm = pe.matmul(uz[:, a:a + CHUNK // P + 1:CHUNK // P], v[:, a * P:(a + 1) * P], pick_chunks[:, :],
                                   start=True, stop=True)
                mm.then_inc(z2_summed, 1)

            def body(i, is_first=False, is_last=False, before_last=False):
                first_k = T0 if is_last else 0
                slots = [Slot(i, k, is_last) for k in range(first_k, SLOTS)]
                after = [] if is_last else [Slot(i + 1, k, before_last) for k in range(T0 if before_last else 0, SLOTS)]
                ahead = slots[AHEAD:] + after[:AHEAD]
                for n, slot in enumerate(slots):
                    if slot.k == 0:
                        pe.wait_ge(h1_ready, 2 * (i + 1))
                        pe.wait_ge(direct0_ready, i + 1)
                    if slot.k == T0 and not is_first:
                        pe.wait_ge(direct1_ready, i)
                        pe.wait_ge(h2_ready, i)
                    for c in range(2):
                        if n < len(ahead):
                            spread(ahead[n], c)
                        if c == 1 and slot.k == T0 + 3 and not is_first:
                            wait_layer2_u(i - 1)
                        contract(slot, c)
                    if not is_first:
                        if slot.k == T0 + 3:
                            layer2_u(i - 1)
                        if slot.k == T0 + 9:
                            layer2_z(i - 1)

            pe.wait_ge(small_loaded, 16 * 6)
            opening = [FirstSlot(k) for k in range(T0)]
            ahead = opening + [Slot(0, k) for k in range(AHEAD)]
            for slot in ahead[:AHEAD]:
                for c in range(2):
                    spread(slot, c)
            pe.wait_ge(w_hi_ready, 2)
            pe.wait_ge(w_lo_ready, 2)
            for n, slot in enumerate(opening):
                for c in range(2):
                    spread(ahead[n + AHEAD], c)
                    contract(slot, c)
            body(0, is_first=True)
            with pe.Fori(1, last - 1) as i:
                body(i)
            body(last - 1, before_last=True)
            body(last, is_last=True)
            wait_layer2_u(last)
            layer2_u(last)
            layer2_z(last)

            pe.wait_ge(final_loaded, 32)
            pe.wait_ge(direct_summed, pairs + 1)
            for r in range(4):
                if r >= 2:
                    pe.wait_ge(res_ready, 2 * (r - 1))
                for half in range(2):
                    rows = slice(half * HALF, (half + 1) * HALF)
                    start = half * B_PAIR + r
                    mm = pe.transpose((acc0, acc1)[half][:, r % 2, 0:HALF],
                                      sums[rows, start:start + samples - 3:4], idents[rows, rows])
                mm.then_inc(turned, 1)
            pe.wait_ge(z2_ready, pairs)
            pe.matmul(xe[:, 2, 0:4], z2[:, :], pick_bs[:, :], start=True, stop=True).then_inc(z2_final, 1)

        @block.vector
        def _(dve):
            dve.memset(w0a[:, 4, :], 0.0).then_inc(w0_zeroed, 1)
            dve.memset(w0b[:, 4, :], 0.0).then_inc(w0_zeroed, 1)
            dve.memset(w0b[0:FIELDS, 0, :], 0.0).then_inc(w0_zeroed, 1)

            def cut(step, late):
                cols = slice(early, q_cols) if late else slice(0, early)
                wait_parts(dve, step + 1, late)
                dve.tensor_tensor(xq[:, cols], xq[:, cols], xq_parts[:, step, cols], ALU.subtract).then_inc(rest_ready, 1)

            cut(0, 0)
            cut(1, 0)
            dve.wait_ge(w0_loaded, 16 * 5)
            dve.tensor_tensor(w0a[:, :, :], w0a[:, :, :], w0b[:, :, :], ALU.add).then_inc(w0_summed, 1)
            dve.wait_ge(w_hi_ready, 1)
            dve.tensor_tensor(w0_lo[:, :, :], w0a[:, :, :], w0_hi[:, :, :].bitcast(F32), ALU.subtract).then_inc(w_lo_ready, 1)
            dve.wait_ge(w_hi_ready, 2)
            dve.tensor_tensor(w1_lo[:, :, :], w1s[:, :, :], w1_hi[:, :, :].bitcast(F32), ALU.subtract).then_inc(w_lo_ready, 1)

            def multiply(slot):
                if not isinstance(slot.done, int) or slot.done > RING:
                    dve.wait_ge(slot_done, slot.done - RING)
                other = h1 if slot.layer1 else x4
                for c in range(2):
                    cols = slice(c * CHUNK, (c + 1) * CHUNK)
                    dve.wait_ge(xe_ready, 2 * slot.before + c + 1)
                    dve.tensor_tensor(prod[:, slot.ring, cols], xe[:, slot.xe[c], :], other[:, cols],
                                      ALU.mult).then_inc(prod_ready, 1)

            def make_lo(slot):
                dve.wait_ge(hi_ready, slot.done)
                dve.tensor_tensor(lo[:, slot.ring, :], prod[:, slot.ring, :], hi[:, slot.ring, :].bitcast(F32),
                                  ALU.subtract).then_inc(lo_vector_ready, 1)

            def slots_of(slots, after):
                for n, slot in enumerate(slots):
                    multiply(slot)
                    if n >= LO_LAG and slots[n - LO_LAG].on_vector:
                        make_lo(slots[n - LO_LAG])
                    after(slot)
                for slot in slots[-LO_LAG:]:
                    if slot.on_vector:
                        make_lo(slot)

            def sum_direct(i, rows):
                dve.tensor_reduce(sums[rows, bass.ds(i * B_PAIR, B_PAIR)],
                                  direct[rows, :].rearrange("p (b d) -> p b d", d=D), AX_X, ALU.add).then_inc(direct_summed, 1)

            def make_v(i):
                dve.wait_ge(xv_loaded, 32 * (i + 1))
                dve.wait_ge(u_ready, i + 1)
                dve.tensor_tensor(v[:, :], uz[0:HALF, :], xv[:, :], ALU.mult).then_inc(v_ready, 1)

            def body(i, is_first=False, is_last=False):
                def after(slot):
                    if slot.k == T0 - 1:
                        dve.wait_ge(h1_ready, 2 * (i + 1))
                    if is_first and slot.k in (T0 + 1, T0 + 4):
                        cut(0 if slot.k == T0 + 1 else 1, 1)
                    if slot.k == T0 + 3:
                        dve.wait_ge(direct0_ready, i + 1)
                        if not is_first:
                            dve.wait_ge(direct1_ready, i)
                        sum_direct(i, slice(0, HALF) if is_first else slice(0, P))
                    if slot.k == T0 + 6 and not is_first:
                        make_v(i - 1)

                if is_last:
                    dve.wait_ge(h1_ready, 2 * (i + 1))
                else:
                    dve.wait_ge(x4_loaded, 64 * (i + 2))
                slots_of([Slot(i, k, is_last) for k in range(T0 if is_last else 0, SLOTS)], after)

            dve.wait_ge(x4_loaded, 64)
            slots_of([FirstSlot(k) for k in range(T0)], lambda slot: None)
            body(0, is_first=True)
            with dve.Fori(1, last) as i:
                body(i)
            body(last, is_last=True)
            dve.wait_ge(direct1_ready, pairs)
            sum_direct(pairs, slice(HALF, P))
            make_v(last)
            for r in range(4):
                dve.wait_ge(turned, r + 1)
                for half, acc in enumerate((acc0, acc1)):
                    dve.tensor_copy(res[:, r, half * HALF:(half + 1) * HALF], acc[:, r % 2, 0:HALF]).then_inc(res_ready, 1)
            dve.wait_ge(z2_final, 1)
            dve.tensor_copy(res[:, :, P:P + 1], xe[:, 2, 0:4].rearrange("p (r a) -> p r a", a=1)).then_inc(res_ready, 1)

        @block.gpsimd
        def _(pool):
            def slots_of(slots):
                for slot in slots:
                    if not slot.on_vector:
                        pool.wait_ge(hi_ready, slot.done)
                        pool.tensor_tensor(lo[:, slot.ring, :], prod[:, slot.ring, :], hi[:, slot.ring, :].bitcast(F32),
                                           ALU.subtract).then_inc(lo_pool_ready, 1)

            slots_of([FirstSlot(k) for k in range(T0)])
            with pool.Fori(0, last) as i:
                slots_of([Slot(i, k) for k in range(SLOTS)])
            slots_of([Slot(last, k, True) for k in range(T0, SLOTS)])

        @block.scalar
        def _(act):
            def part(step, late):
                cols = slice(early, q_cols) if late else slice(0, early)
                if step:
                    act.wait_ge(rest_ready, step + 2 * late)
                else:
                    act.wait_ge(xq_late_loaded if late else xq_loaded, 64)
                act.activation(xq_parts[:, step, cols], xq[:, cols], ACT.Copy).then_inc(part_ready, 1)

            for step in range(PARTS):
                part(step, 0)
            act.wait_ge(w0_summed, 1)
            act.activation(w0_hi[:, :, :], w0a[:, :, :], ACT.Copy).then_inc(w_hi_ready, 1)
            act.wait_ge(w1_loaded, 16)
            act.activation(w1_hi[:, :, :], w1s[:, :, :], ACT.Copy).then_inc(w_hi_ready, 1)
            act.wait_ge(small_loaded, 16 * 6)

            def make_hi(slot):
                act.wait_ge(prod_ready, 2 * slot.done)
                act.activation(hi[:, slot.ring, :], prod[:, slot.ring, :], ACT.Copy).then_inc(hi_ready, 1)

            def leave_layer0(i, done, is_first=False):
                act.wait_ge(slot_done, done)
                if not is_first:
                    act.wait_ge(prod_ready, 2 * (T0 + SLOTS * i))
                for half in range(2):
                    act.activation(h1[half * HALF:(half + 1) * HALF, :],
                                   acc0[0:HALF, :, :].rearrange("p c n -> p (c n)"), ACT.Relu,
                                   bias=b0s[0:HALF, :]).then_inc(h1_ready, 1)
                if not is_first:
                    act.wait_ge(direct_summed, i)
                act.activation(direct[0:HALF, :], acc0[HALF:P, :, :].rearrange("p c n -> p (c n)"), ACT.Relu,
                               bias=b0s[HALF:P, :]).then_inc(direct0_ready, 1)

            def leave_layer1(i, done):
                act.wait_ge(slot_done, done)
                act.wait_ge(direct_summed, i + 1)
                act.activation(h2[:, :], acc1[0:HALF, :, :].rearrange("p c n -> p (c n)"), ACT.Relu,
                               bias=b1s[0:HALF, :]).then_inc(h2_ready, 1)
                act.activation(direct[HALF:P, :], acc1[HALF:P, :, :].rearrange("p c n -> p (c n)"), ACT.Relu,
                               bias=b1s[HALF:P, :]).then_inc(direct1_ready, 1)

            def leave_layer2(i):
                act.wait_ge(z2_summed, i + 1)
                act.activation(z2[:, bass.ds(i * Z2_COLS, Z2_COLS)], uz[:, 0:Z2_COLS], ACT.Relu,
                               bias=b2s[:, :]).then_inc(z2_ready, 1)

            def body(i, is_first=False, is_last=False):
                leave_layer0(i, T0 if is_first else T0 + SLOTS * (i - 1) + T0, is_first)
                for slot in [Slot(i, k, is_last) for k in range(T0 if is_last else 0, SLOTS)]:
                    make_hi(slot)
                    if not is_first and slot.k == (T0 if is_last else T0 - 2):
                        leave_layer1(i - 1, T0 + SLOTS * i)
                    if not is_first and slot.k == T0 + 12:
                        leave_layer2(i - 1)
                    if is_first and slot.k in (T0, T0 + 3, T0 + 6):
                        part((slot.k - T0) // 3, 1)

            for k in range(T0):
                make_hi(FirstSlot(k))
            body(0, is_first=True)
            with act.Fori(1, last) as i:
                body(i)
            body(last, is_last=True)
            leave_layer1(last, T0 + SLOTS * last + T1)
            leave_layer2(last)


def kernel(r_x, L0_rec_W0, L0_rec_b0, L0_rec_W1, L0_rec_b1, L0_rec_W2, L0_rec_b2):
    import numpy as np
    import ml_dtypes
    import concourse.bacc as bacc
    from concourse.bass_utils import run_bass_kernel_spmd

    samples, fields, d = r_x.shape
    x = np.ascontiguousarray(np.asarray(r_x).transpose(1, 0, 2)).reshape(fields, samples * d)
    w0 = np.asarray(L0_rec_W0).reshape(P, fields, fields)
    pairs = [(m, (m + s) % fields) for s in range(17) for m in range(fields if s < 16 else fields // 2)]
    a, b = np.array(pairs).T
    straight = np.ascontiguousarray(w0[:, a, b].T)
    mirrored = np.ascontiguousarray(w0[:, b[fields:], a[fields:]].T)
    w1 = np.asarray(L0_rec_W1).reshape(P, HALF, T1, 2).transpose(3, 1, 2, 0)
    w1 = np.ascontiguousarray(w1).reshape(P, T1, P)

    sel = np.zeros((PARTS, fields, SLOTS, P), np.float32)
    for row, (_, m2) in enumerate(pairs):
        sel[:, m2, row // P, row % P] = 1
    for t in range(T1):
        for half in range(2):
            sel[:, 2 * t + half, T0 + t, half * HALF:(half + 1) * HALF] = 1
    sel = sel.reshape(PARTS * fields, SLOTS, P).astype(ml_dtypes.bfloat16)
    ident = np.eye(P, dtype=np.float32)
    pick_chunk = np.repeat(np.eye(2, dtype=np.float32), fields, axis=0)
    pick_b = np.repeat(np.eye(4, dtype=np.float32), d, axis=0)

    arrays = {
        "x": x, "w0_straight": straight, "w0_mirrored": mirrored,
        "b0": np.asarray(L0_rec_b0).reshape(P, 1), "w1": w1, "b1": np.asarray(L0_rec_b1).reshape(P, 1),
        "w2": np.asarray(L0_rec_W2), "b2": np.ascontiguousarray(np.broadcast_to(np.asarray(L0_rec_b2).reshape(1, 1), (P, 1))),
        "sel": sel, "ident": ident, "pick_chunk": pick_chunk, "pick_b": pick_b,
    }
    nc = bacc.Bacc("TRN2", target_bir_lowering=False, num_devices=1)
    ins = {n: nc.dram_tensor(f"in_{n}", v.shape, mybir.dt.from_np(v.dtype), kind="ExternalInput").ap()
           for n, v in arrays.items()}
    out = nc.dram_tensor("out_0", (samples, P + 1), F32, kind="ExternalOutput").ap()
    cin_kernel(nc, *ins.values(), out)
    r = run_bass_kernel_spmd(nc, [{f"in_{n}": v for n, v in arrays.items()}], core_ids=[0])
    return r.results[0]["out_0"]
```

```python
from contextlib import ExitStack

import concourse.bass as bass
from concourse import mybir

F32 = mybir.dt.float32
F32R = mybir.dt.float32r
BF16 = mybir.dt.bfloat16
ALU = mybir.AluOpType
ACT = mybir.ActivationFunctionType
AX_X = mybir.AxisListType.X

P = 128
FIELDS = 32
D = 32
CHUNK = 512
PAIR = 2 * CHUNK
HALF = 64
T0 = 5
T1 = 16
SLOTS = T0 + T1
SYM_ROWS = 16 * FIELDS + FIELDS // 2
PARTS = 3
RING = 7
AHEAD = 4
GROUP = 4
LO_ON_VECTOR = (1, 4, 7, 9, 14, 16, 19)
LO_LAG = 2
B_PAIR = PAIR // D
LAYER2_TILE = 5
BLOCKS = PAIR // P
Q = PAIR // 4
STACKED = T0 - 1
PARTS_AT = {T0 + 5 * g + 2 * step: (step, g + 1) for g in range(3) for step in range(PARTS)}
CUTS = {T0 + 5 * g + 2 * step + 1: (step, g + 1) for g in range(3) for step in range(PARTS - 1)}


def count_lo(k, on_vector, first=0):
    return sum((s in LO_ON_VECTOR) == on_vector for s in range(first, k + 1))


class Slot:

    def __init__(self, i, k, last=False):
        first = T0 if last else 0
        self.k, self.i = k, i
        self.layer1 = k >= T0
        self.pair = i if self.layer1 else i + 1
        self.tile = k - T0 if self.layer1 else k
        self.before = T0 + SLOTS * i + (k - first)
        self.done = self.before + 1
        self.ring = (T0 + (SLOTS * i if last else 0) + k - first) % RING
        if self.layer1 and self.tile < 2:
            self.spread_free = None if isinstance(i, int) and i == 0 else self.before - 1 - (T0 - first)
        else:
            self.spread_free = self.before - 1
        self.on_vector = k in LO_ON_VECTOR
        self.stacked = k == STACKED
        self.lo = (count_lo(T0 - 1, self.on_vector) + count_lo(SLOTS - 1, self.on_vector) * i
                   + count_lo(k, self.on_vector, first))


class FirstSlot(Slot):

    def __init__(self, k):
        self.k, self.layer1, self.pair, self.tile = k, False, 0, k
        self.before, self.done = k, k + 1
        self.ring = k % RING
        self.on_vector = k in LO_ON_VECTOR
        self.stacked = k == STACKED
        self.lo = count_lo(k, self.on_vector)


def cin_kernel(nc, x, x_wrapped, x_cols, w0_straight, w0_mirrored, b0, w1, b1, w2, b2, sel, ident, pick_b, out):
    n_cols = x.shape[1]
    pairs = n_cols // PAIR
    last = pairs - 1
    q_cols = n_cols // 4
    group_cols = GROUP * Q
    samples = n_cols // D

    with ExitStack() as ctx:
        def sb(name, shape, dt=F32):
            return ctx.enter_context(nc.sbuf_tensor(name, shape, dt))

        def psum(name, shape):
            return ctx.enter_context(nc.psum_tensor(name, shape, F32))

        def sem(name):
            return ctx.enter_context(nc.semaphore(name))

        w0a = sb("w0a", [P, T0, P])
        w0b = sb("w0b", [P, T0, P])
        w1s = sb("w1s", [P, T1, P])
        w0_hi = sb("w0_hi", [P, T0, P], F32R)
        w0_lo = sb("w0_lo", [P, STACKED, P], F32R)
        w1_hi = sb("w1_hi", [P, T1, P], F32R)
        w1_lo = sb("w1_lo", [P, T1, P], F32R)
        w2s = sb("w2s", [HALF, FIELDS])
        b0s = sb("b0s", [P, 1])
        b1s = sb("b1s", [P, 1])
        b2s = sb("b2s", [P, 1])
        sels = sb("sels", [PARTS * FIELDS, T1, P], BF16)
        idents = sb("idents", [P, P])
        pick_bs = sb("pick_bs", [P, 4])
        xq = sb("xq", [P, 2, group_cols])
        xq_parts = sb("xq_parts", [P, PARTS, group_cols], BF16)
        xp = sb("xp", [PARTS * FIELDS, PAIR], BF16)
        x4 = sb("x4", [P, PAIR])
        x_shifted = sb("x_shifted", [P, T0, PAIR])
        xt = sb("xt", [P, n_cols // P * FIELDS])
        prod = sb("prod", [P, RING, PAIR])
        hi = sb("hi", [P, RING, PAIR], F32R)
        lo = sb("lo", [P, RING, PAIR], F32R)
        h1 = sb("h1", [P, PAIR])
        h2 = sb("h2", [HALF, PAIR])
        direct = sb("direct", [P, PAIR])
        sums = sb("sums", [P, samples + B_PAIR])
        v = sb("v", [P, BLOCKS * FIELDS])
        z2_in = sb("z2_in", [P, BLOCKS * pairs])
        z2 = sb("z2", [P, BLOCKS * pairs])
        res = sb("res", [P, 4, P + 1])
        xe = psum("xe", [P, 2, 2, CHUNK])
        acc0 = psum("acc0", [P, 2, CHUNK])
        acc1 = psum("acc1", [P, 2, CHUNK])

        parts_dram = nc.dram_tensor("parts_scratch", (P, PARTS, q_cols), BF16, kind="Internal").ap()

        x_shifted_zeroed = sem("x_shifted_zeroed")
        w0_loaded = sem("w0_loaded")
        w1_loaded = sem("w1_loaded")
        small_loaded = sem("small_loaded")
        final_loaded = sem("final_loaded")
        w0_summed = sem("w0_summed")
        w_hi_ready = sem("w_hi_ready")
        w_lo_ready = sem("w_lo_ready")
        xq_loaded = [sem(f"xq_loaded{place}") for place in range(2)]
        part_ready = sem("part_ready")
        rest_ready = sem("rest_ready")
        parts_stored = sem("parts_stored")
        xp_loaded = sem("xp_loaded")
        layer0_loaded = sem("layer0_loaded")
        xt_loaded = sem("xt_loaded")
        xe_ready = sem("xe_ready")
        prod_ready = sem("prod_ready")
        hi_ready = sem("hi_ready")
        lo_vector_ready = sem("lo_vector_ready")
        lo_pool_ready = sem("lo_pool_ready")
        slot_done = sem("slot_done")
        h1_ready = sem("h1_ready")
        direct0_ready = sem("direct0_ready")
        direct1_ready = sem("direct1_ready")
        h2_ready = sem("h2_ready")
        direct_summed = sem("direct_summed")
        u_ready = sem("u_ready")
        v_ready = sem("v_ready")
        z2_summed = sem("z2_summed")
        z2_ready = sem("z2_ready")
        turned = sem("turned")
        z2_final = sem("z2_final")
        res_ready = sem("res_ready")
        stored = sem("stored")

        block = ctx.enter_context(nc.Block())

        x_q = x.rearrange("m (q j i) -> j m q i", j=4, i=Q)
        parts_q = parts_dram.rearrange("(j m) r n -> r m j n", j=4)
        n_groups = pairs // GROUP
        layer0_dmas = 4 + 4 + 3

        @block.sync
        def _(sp):
            def load_xq(g):
                if g >= 2:
                    sp.wait_ge(part_ready, PARTS * (g - 1))
                for j in range(4):
                    sp.dma_start(xq[j * FIELDS:(j + 1) * FIELDS, g % 2, :].rearrange("p (q i) -> p q i", i=Q),
                                 x_q[j][:, g * GROUP:(g + 1) * GROUP, :]).then_inc(xq_loaded[g % 2], 16)

            def load_parts(q):
                for r in range(PARTS):
                    sp.dma_start(xp[r * FIELDS:(r + 1) * FIELDS, :].rearrange("p (j i) -> p j i", i=Q),
                                 parts_q[r][:, :, bass.ds(q * Q, Q)]).then_inc(xp_loaded, 16)

            def load_layer0(q):
                cols = bass.ds(q * PAIR, PAIR)
                for j in range(4):
                    rows = slice(j * FIELDS, (j + 1) * FIELDS)
                    sp.dma_start(x4[rows, :], x[:, cols]).then_inc(layer0_loaded, 16)
                    for_tiles = bass.AP(x_wrapped.tensor, j * n_cols, [[n_cols, FIELDS], [4 * n_cols, STACKED], [1, n_cols]])
                    sp.dma_start(x_shifted[rows, 0:STACKED, :], for_tiles[:, :, cols]).then_inc(layer0_loaded, 16)
                    if j < 3:
                        rest = slice(j * FIELDS, j * FIELDS + FIELDS // 2)
                        sp.dma_start(x_shifted[rest, STACKED, :], x[FIELDS // 2:, cols]).then_inc(layer0_loaded, 16)

            sp.wait_ge(x_shifted_zeroed, 1)
            load_layer0(0)
            sp.dma_start(w0a[:, :, :], w0_straight).then_inc(w0_loaded, 16)
            sp.dma_start(w0b[:, :, :], w0_mirrored).then_inc(w0_loaded, 16)
            load_xq(0)
            sp.dma_start(w1s[:, :, :], w1).then_inc(w1_loaded, 16)
            sp.dma_start(b0s[:, :], b0).then_inc(small_loaded, 16)
            sp.dma_start(b1s[:, :], b1).then_inc(small_loaded, 16)
            sp.dma_start(w2s[:, :], w2.rearrange("a (h m) -> (a h) m", m=FIELDS)).then_inc(small_loaded, 16)
            sp.dma_start(b2s[:, :], b2).then_inc(small_loaded, 16)
            sp.dma_start(sels[:, :, :], sel).then_inc(small_loaded, 16)
            sp.wait_ge(parts_stored, 16)
            load_parts(0)
            sp.wait_ge(prod_ready, T0)
            load_layer0(1)
            load_xq(1)
            load_xq(2)
            sp.dma_start(xt[:, :], x_cols).then_inc(xt_loaded, 16)
            sp.dma_start(idents[:, :], ident).then_inc(final_loaded, 16)
            sp.dma_start(pick_bs[:, :], pick_b).then_inc(final_loaded, 16)
            load_xq(3)

            def refill(q):
                sp.wait_ge(prod_ready, T0 + SLOTS * (q - 2) + T0)
                load_layer0(q)
                sp.wait_ge(xe_ready, T1 * (q - 1))
                load_parts(q - 1)

            refill(2)
            sp.wait_ge(parts_stored, 16 * n_groups)
            with sp.Fori(3, pairs) as q:
                refill(q)
            sp.wait_ge(xe_ready, T1 * last)
            load_parts(last)
            sp.wait_ge(res_ready, 9)
            sp.dma_start(out.rearrange("(q r) c -> q r c", r=4), res[:, :, :]).then_inc(stored, 16)
            sp.wait_ge(stored, 16)

        @block.tensor
        def _(pe):
            def spread(slot):
                if slot.tile == 0:
                    pe.wait_ge(xp_loaded, 16 * PARTS * (slot.pair + 1))
                if slot.spread_free is not None:
                    pe.wait_ge(prod_ready, slot.spread_free)
                for c in range(2):
                    mm = pe.matmul(xe[:, slot.tile % 2, c, :], sels[:, slot.tile, :], xp[:, c * CHUNK:(c + 1) * CHUNK],
                                   start=True, stop=True)
                mm.then_inc(xe_ready, 1)

            def contract(slot, c):
                acc = acc1 if slot.layer1 else acc0
                w_hi, w_lo, tiles = (w1_hi, w1_lo, T1) if slot.layer1 else (w0_hi, w0_lo, T0)
                cols = slice(c * CHUNK, (c + 1) * CHUNK)
                if c == 0:
                    pe.wait_ge(hi_ready, slot.done)
                    if slot.stacked:
                        pe.wait_ge(lo_vector_ready if slot.on_vector else lo_pool_ready, slot.lo)
                first, final = slot.tile == 0, slot.tile == tiles - 1
                if slot.stacked:
                    mm = pe.matmul(acc[:, c, :], w_hi[:, slot.tile, :], hi[:, slot.ring, cols], start=False, stop=True)
                    if c == 1:
                        mm.then_inc(slot_done, 1)
                    return
                pe.matmul(acc[:, c, :], w_hi[:, slot.tile, :], hi[:, slot.ring, cols], start=first, stop=False)
                pe.matmul(acc[:, c, :], w_lo[:, slot.tile, :], hi[:, slot.ring, cols], start=False, stop=False)
                if c == 0:
                    pe.wait_ge(lo_vector_ready if slot.on_vector else lo_pool_ready, slot.lo)
                mm = pe.matmul(acc[:, c, :], w_hi[:, slot.tile, :], lo[:, slot.ring, cols], start=False, stop=final)
                if c == 1:
                    mm.then_inc(slot_done, 1)

            def layer2(i, place, free):
                pe.wait_ge(prod_ready, free)
                pe.wait_ge(h2_ready, i + 1)
                for a in range(BLOCKS):
                    mm = pe.matmul(xe[:, place, 0, a * FIELDS:(a + 1) * FIELDS], h2[:, a * P:(a + 1) * P], w2s[:, :],
                                   start=True, stop=True)
                mm.then_inc(u_ready, 1)

            def body(i, is_first=False, is_last=False, before_last=False):
                first_k = T0 if is_last else 0
                slots = [Slot(i, k, is_last) for k in range(first_k, SLOTS)]
                after = [] if is_last else [Slot(i + 1, k, before_last) for k in range(T0 if before_last else 0, SLOTS)]
                ahead = slots[AHEAD:] + after[:AHEAD]
                for n, slot in enumerate(slots):
                    if slot.k == 0:
                        pe.wait_ge(h1_ready, 2 * (i + 1))
                        pe.wait_ge(direct0_ready, i + 1)
                    if slot.k == T0 and not is_first:
                        pe.wait_ge(direct1_ready, i)
                        pe.wait_ge(h2_ready, i)
                    if n < len(ahead) and ahead[n].layer1:
                        if slot.layer1 and slot.tile == LAYER2_TILE + 1 and not is_first:
                            pe.wait_ge(v_ready, i)
                        spread(ahead[n])
                    for c in range(2):
                        contract(slot, c)
                    if slot.layer1 and slot.tile == LAYER2_TILE and not is_first:
                        layer2(i - 1, (slot.tile + 1 + AHEAD) % 2, slot.done + AHEAD - 1)

            pe.wait_ge(w_hi_ready, 1)
            pe.wait_ge(w_lo_ready, 2)
            opening = [FirstSlot(k) for k in range(T0)]
            for slot in opening:
                for c in range(2):
                    contract(slot, c)
            pe.wait_ge(w_hi_ready, 2)
            pe.wait_ge(w_lo_ready, 3)
            pe.wait_ge(small_loaded, 16 * 5)
            body(0, is_first=True)
            with pe.Fori(1, last - 1) as i:
                body(i)
            body(last - 1, before_last=True)
            body(last, is_last=True)
            layer2(last, 0, T0 + SLOTS * last + T1)

            pe.wait_ge(final_loaded, 32)
            pe.wait_ge(direct_summed, pairs + 1)
            for r in range(4):
                if r >= 2:
                    pe.wait_ge(res_ready, 2 * (r - 1))
                for half in range(2):
                    rows = slice(half * HALF, (half + 1) * HALF)
                    start = half * B_PAIR + r
                    mm = pe.transpose((acc0, acc1)[half][:, r % 2, 0:HALF],
                                      sums[rows, start:start + samples - 3:4], idents[rows, rows])
                mm.then_inc(turned, 1)
            pe.wait_ge(z2_ready, 1)
            pe.matmul(xe[:, 1, 0, 0:4], z2[:, :], pick_bs[:, :], start=True, stop=True).then_inc(z2_final, 1)

        @block.vector
        def _(dve):
            dve.memset(x_shifted[:, STACKED, :], 0.0).then_inc(x_shifted_zeroed, 1)

            def cut(step, g):
                dve.wait_ge(part_ready, PARTS * g + step + 1)
                dve.tensor_tensor(xq[:, g % 2, :], xq[:, g % 2, :], xq_parts[:, step, :], ALU.subtract).then_inc(rest_ready, 1)

            dve.wait_ge(w0_loaded, 32)
            dve.tensor_tensor(w0a[:, :, :], w0a[:, :, :], w0b[:, :, :], ALU.add).then_inc(w0_summed, 1)
            dve.wait_ge(w_hi_ready, 1)
            dve.tensor_tensor(w0_lo[:, :, :], w0a[:, 0:STACKED, :], w0_hi[:, 0:STACKED, :].bitcast(F32), ALU.subtract).then_inc(w_lo_ready, 1)
            mid = slice(FIELDS, 2 * FIELDS)
            dve.tensor_tensor(w0_hi[mid, STACKED, :], w0a[mid, STACKED, :], w0_hi[mid, STACKED, :].bitcast(F32),
                              ALU.subtract).then_inc(w_lo_ready, 1)

            def multiply(slot):
                if not isinstance(slot.done, int) or slot.done > RING:
                    dve.wait_ge(slot_done, slot.done - RING)
                if slot.layer1:
                    dve.wait_ge(xe_ready, T1 * slot.pair + slot.tile + 1)
                    spread = xe[:, slot.tile % 2, :, :].rearrange("p c n -> p (c n)")
                    dve.tensor_tensor(prod[:, slot.ring, :], spread, h1[:, :], ALU.mult).then_inc(prod_ready, 1)
                else:
                    dve.tensor_tensor(prod[:, slot.ring, :], x_shifted[:, slot.tile, :], x4[:, :],
                                      ALU.mult).then_inc(prod_ready, 1)

            def make_lo(slot):
                dve.wait_ge(hi_ready, slot.done)
                rows = slice(2 * FIELDS, 3 * FIELDS) if slot.stacked else slice(0, P)
                to = hi if slot.stacked else lo
                dve.tensor_tensor(to[rows, slot.ring, :], prod[rows, slot.ring, :], hi[rows, slot.ring, :].bitcast(F32),
                                  ALU.subtract).then_inc(lo_vector_ready, 1)

            def slots_of(slots, after):
                for n, slot in enumerate(slots):
                    multiply(slot)
                    if n >= LO_LAG and slots[n - LO_LAG].on_vector:
                        make_lo(slots[n - LO_LAG])
                    after(slot)
                for slot in slots[-LO_LAG:]:
                    if slot.on_vector:
                        make_lo(slot)

            def sum_direct(i, rows):
                dve.tensor_reduce(sums[rows, bass.ds(i * B_PAIR, B_PAIR)],
                                  direct[rows, :].rearrange("p (b d) -> p b d", d=D), AX_X, ALU.add).then_inc(direct_summed, 1)

            def layer2(i, place):
                dve.wait_ge(u_ready, i + 1)
                dve.tensor_tensor(v[:, :], xe[:, place, 0, 0:BLOCKS * FIELDS],
                                  xt[:, bass.ds(i * (BLOCKS * FIELDS), BLOCKS * FIELDS)], ALU.mult).then_inc(v_ready, 1)
                dve.wait_ge(v_ready, i + 1)
                dve.tensor_reduce(z2_in[:, bass.ds(i * BLOCKS, BLOCKS)], v[:, :].rearrange("p (a m) -> p a m", m=FIELDS),
                                  AX_X, ALU.add).then_inc(z2_summed, 1)

            def body(i, is_first=False, is_last=False):
                def after(slot):
                    if slot.k == T0 - 1:
                        dve.wait_ge(h1_ready, 2 * (i + 1))
                    if is_first and slot.k in CUTS:
                        cut(*CUTS[slot.k])
                    if slot.layer1 and slot.tile == LAYER2_TILE + AHEAD:
                        dve.wait_ge(direct0_ready, i + 1)
                        if not is_first:
                            dve.wait_ge(direct1_ready, i)
                        sum_direct(i, slice(0, HALF) if is_first else slice(0, P))
                        if not is_first:
                            layer2(i - 1, (slot.tile + 1) % 2)

                if is_last:
                    dve.wait_ge(h1_ready, 2 * (i + 1))
                else:
                    dve.wait_ge(layer0_loaded, 16 * layer0_dmas * (i + 2))
                slots_of([Slot(i, k, is_last) for k in range(T0 if is_last else 0, SLOTS)], after)

            dve.wait_ge(layer0_loaded, 16 * layer0_dmas)
            slots_of([FirstSlot(k) for k in range(T0)], lambda slot: None)
            cut(0, 0)
            dve.wait_ge(w_hi_ready, 2)
            dve.tensor_tensor(w1_lo[:, :, :], w1s[:, :, :], w1_hi[:, :, :].bitcast(F32), ALU.subtract).then_inc(w_lo_ready, 1)
            cut(1, 0)
            body(0, is_first=True)
            dve.wait_ge(xt_loaded, 16)
            with dve.Fori(1, last) as i:
                body(i)
            body(last, is_last=True)
            dve.wait_ge(direct1_ready, pairs)
            sum_direct(pairs, slice(HALF, P))
            layer2(last, 0)
            for r in range(4):
                dve.wait_ge(turned, r + 1)
                for half, acc in enumerate((acc0, acc1)):
                    dve.tensor_copy(res[:, r, half * HALF:(half + 1) * HALF], acc[:, r % 2, 0:HALF]).then_inc(res_ready, 1)
            dve.wait_ge(z2_final, 1)
            dve.tensor_copy(res[:, :, P:P + 1], xe[:, 1, 0, 0:4].rearrange("p (r a) -> p r a", a=1)).then_inc(res_ready, 1)

        @block.gpsimd
        def _(pool):
            def slots_of(slots):
                for slot in slots:
                    if not slot.on_vector:
                        pool.wait_ge(hi_ready, slot.done)
                        pool.tensor_tensor(lo[:, slot.ring, :], prod[:, slot.ring, :], hi[:, slot.ring, :].bitcast(F32),
                                           ALU.subtract).then_inc(lo_pool_ready, 1)

            slots_of([FirstSlot(k) for k in range(T0)])
            with pool.Fori(0, last) as i:
                slots_of([Slot(i, k) for k in range(SLOTS)])
            slots_of([Slot(last, k, True) for k in range(T0, SLOTS)])

        @block.scalar
        def _(act):
            def part(step, g):
                if step:
                    act.wait_ge(rest_ready, step + 2 * g)
                else:
                    act.wait_ge(xq_loaded[g % 2], 64 * (g // 2 + 1))
                    if g:
                        act.wait_ge(parts_stored, 16 * g)
                act.activation(xq_parts[:, step, :], xq[:, g % 2, :], ACT.Copy).then_inc(part_ready, 1)

            def store_parts(g):
                act.wait_ge(part_ready, PARTS * (g + 1))
                act.dma_start(parts_dram[:, :, g * group_cols:(g + 1) * group_cols], xq_parts[:, :, :]).then_inc(parts_stored, 16)

            act.wait_ge(w0_summed, 1)
            act.activation(w0_hi[:, :, :], w0a[:, :, :], ACT.Copy).then_inc(w_hi_ready, 1)

            def make_hi(slot):
                act.wait_ge(prod_ready, slot.done)
                act.activation(hi[:, slot.ring, :], prod[:, slot.ring, :], ACT.Copy).then_inc(hi_ready, 1)

            def leave_layer0(i, done, is_first=False):
                act.wait_ge(slot_done, done)
                if not is_first:
                    act.wait_ge(prod_ready, T0 + SLOTS * i)
                for half in range(2):
                    act.activation(h1[half * HALF:(half + 1) * HALF, :],
                                   acc0[0:HALF, :, :].rearrange("p c n -> p (c n)"), ACT.Relu,
                                   bias=b0s[0:HALF, :]).then_inc(h1_ready, 1)
                if not is_first:
                    act.wait_ge(direct_summed, i)
                act.activation(direct[0:HALF, :], acc0[HALF:P, :, :].rearrange("p c n -> p (c n)"), ACT.Relu,
                               bias=b0s[HALF:P, :]).then_inc(direct0_ready, 1)

            def leave_layer1(i, done):
                act.wait_ge(slot_done, done)
                act.wait_ge(direct_summed, i + 1)
                act.activation(h2[:, :], acc1[0:HALF, :, :].rearrange("p c n -> p (c n)"), ACT.Relu,
                               bias=b1s[0:HALF, :]).then_inc(h2_ready, 1)
                act.activation(direct[HALF:P, :], acc1[HALF:P, :, :].rearrange("p c n -> p (c n)"), ACT.Relu,
                               bias=b1s[HALF:P, :]).then_inc(direct1_ready, 1)

            def body(i, is_first=False, is_last=False):
                leave_layer0(i, T0 if is_first else T0 + SLOTS * (i - 1) + T0, is_first)
                for slot in [Slot(i, k, is_last) for k in range(T0 if is_last else 0, SLOTS)]:
                    make_hi(slot)
                    if not is_first and slot.k == (T0 if is_last else T0 - 2):
                        leave_layer1(i - 1, T0 + SLOTS * i)
                    if is_first and slot.k - 1 in PARTS_AT and PARTS_AT[slot.k - 1][0] == PARTS - 1:
                        store_parts(PARTS_AT[slot.k - 1][1])
                    if is_first and slot.k in PARTS_AT:
                        part(*PARTS_AT[slot.k])

            for k in range(T0):
                make_hi(FirstSlot(k))
                if k == 1:
                    part(0, 0)
            act.wait_ge(w1_loaded, 16)
            act.activation(w1_hi[:, :, :], w1s[:, :, :], ACT.Copy).then_inc(w_hi_ready, 1)
            part(1, 0)
            part(2, 0)
            store_parts(0)
            act.wait_ge(small_loaded, 16 * 5)
            body(0, is_first=True)
            with act.Fori(1, last) as i:
                body(i)
            body(last, is_last=True)
            leave_layer1(last, T0 + SLOTS * last + T1)
            act.wait_ge(z2_summed, pairs)
            act.activation(z2[:, :], z2_in[:, :], ACT.Relu, bias=b2s[:, :]).then_inc(z2_ready, 1)


def kernel(r_x, L0_rec_W0, L0_rec_b0, L0_rec_W1, L0_rec_b1, L0_rec_W2, L0_rec_b2):
    import numpy as np
    import ml_dtypes
    import concourse.bacc as bacc
    from concourse.bass_utils import run_bass_kernel_spmd

    samples, fields, d = r_x.shape
    x = np.ascontiguousarray(np.asarray(r_x).transpose(1, 0, 2)).reshape(fields, samples * d)
    x_cols = np.ascontiguousarray(x.reshape(fields, -1, P).transpose(2, 1, 0)).reshape(P, -1)
    w0 = np.asarray(L0_rec_W0).reshape(P, fields, fields)
    straight = np.zeros((P, T0, P), w0.dtype)
    mirrored = np.zeros((P, T0, P), w0.dtype)
    for s in range(17):
        m = np.arange(fields if s < 16 else fields // 2)
        for copy in range(3 if s == 16 else 1):
            rows = (s % 4 + copy) * fields + m
            straight[rows, s // 4] = w0[:, m, (m + s) % fields].T
            if s:
                mirrored[rows, s // 4] = w0[:, (m + s) % fields, m].T
    w1 = np.asarray(L0_rec_W1).reshape(P, HALF, T1, 2).transpose(3, 1, 2, 0)
    w1 = np.ascontiguousarray(w1).reshape(P, T1, P)

    sel = np.zeros((PARTS, fields, T1, P), np.float32)
    for t in range(T1):
        for half in range(2):
            sel[:, 2 * t + half, t, half * HALF:(half + 1) * HALF] = 1
    sel = sel.reshape(PARTS * fields, T1, P).astype(ml_dtypes.bfloat16)
    ident = np.eye(P, dtype=np.float32)
    pick_b = np.repeat(np.eye(4, dtype=np.float32), d, axis=0)

    arrays = {
        "x": x, "x_wrapped": np.concatenate([x, x[:fields // 2]]), "x_cols": x_cols, "w0_straight": straight, "w0_mirrored": mirrored,
        "b0": np.asarray(L0_rec_b0).reshape(P, 1), "w1": w1, "b1": np.asarray(L0_rec_b1).reshape(P, 1),
        "w2": np.asarray(L0_rec_W2), "b2": np.ascontiguousarray(np.broadcast_to(np.asarray(L0_rec_b2).reshape(1, 1), (P, 1))),
        "sel": sel, "ident": ident, "pick_b": pick_b,
    }
    nc = bacc.Bacc("TRN2", target_bir_lowering=False, num_devices=1)
    ins = {n: nc.dram_tensor(f"in_{n}", v.shape, mybir.dt.from_np(v.dtype), kind="ExternalInput").ap()
           for n, v in arrays.items()}
    out = nc.dram_tensor("out_0", (samples, P + 1), F32, kind="ExternalOutput").ap()
    cin_kernel(nc, *ins.values(), out)
    r = run_bass_kernel_spmd(nc, [{f"in_{n}": v for n, v in arrays.items()}], core_ids=[0])
    return r.results[0]["out_0"]
```

```python
from contextlib import ExitStack

import concourse.bass as bass
from concourse import mybir

F32 = mybir.dt.float32
F32R = mybir.dt.float32r
BF16 = mybir.dt.bfloat16
ALU = mybir.AluOpType
ACT = mybir.ActivationFunctionType
AX_X = mybir.AxisListType.X

P = 128
FIELDS = 32
D = 32
CHUNK = 512
PAIR = 2 * CHUNK
HALF = 64
T0 = 5
T1 = 16
SLOTS = T0 + T1
PARTS = 3
RING = 7
AHEAD = 5
WHOLE = (5, 8, 11, 13, 16, 18)
WHOLE_LAST = (5, 6, 7, 9, 11, 13, 16, 18)
DMA_TILES = (0, 2, 4, 6, 8, 10, 12, 14, 15)
SPREAD_TILES = tuple(t for t in range(T1) if t not in DMA_TILES)
XS_RING = 3
LO_ON_VECTOR = (4,)
LO_LAG = 2
B_PAIR = PAIR // D
U_AT = 14
V_AT = 19
V_SUM_AT = 20
X4_AT = 19
HIDDEN0_AT = {0: (0, 1), 1: (2, 3)}
SUM_AT = 14
BLOCKS = PAIR // P
Q = PAIR // 4
STACKED = T0 - 1
ROUND_AT = {8: 0, 10: 1, 12: 2}
REST_AT = {9: 0, 11: 1}
W1_HI_AT = 4
W1_LO_AT = {1: 0, 6: 1}
DIRECT0_AT = 18
LAYER1_AT = 4


def count_hi(k, first=0, whole=WHOLE):
    return sum(s not in whole for s in range(first, k + 1))


def count_lo(k, on_vector, first=0, whole=WHOLE):
    return sum((s in LO_ON_VECTOR) == on_vector for s in range(first, k + 1) if s not in whole)


class Slot:

    def __init__(self, i, k, last=False):
        first = T0 if last else 0
        self.k, self.i = k, i
        self.layer1 = k >= T0
        self.pair = i if self.layer1 else i + 1
        self.acc = 0 if last or not self.layer1 else 1
        self.tile = k - T0 if self.layer1 else k
        self.before = T0 + SLOTS * i + (k - first)
        self.done = self.before + 1
        self.ring = (T0 + (SLOTS * i if last else 0) + k - first) % RING
        if self.layer1 and self.tile in DMA_TILES:
            n = DMA_TILES.index(self.tile)
            self.dma_place = n % XS_RING
            self.dma_loads = len(DMA_TILES) // XS_RING * i + n // XS_RING + 1
        self.by_tensor = self.layer1 and self.tile in SPREAD_TILES
        if self.by_tensor:
            n = SPREAD_TILES.index(self.tile)
            self.spreads = len(SPREAD_TILES) * i + n + 1
            self.spread_free = (self.before - self.tile if n == 0 else self.done - self.tile + SPREAD_TILES[n - 1])
            if isinstance(i, int) and i == 0 and n == 0:
                self.spread_free = None
        whole = WHOLE_LAST if last else WHOLE
        self.whole = k in whole or (isinstance(i, int) and i == 0 and k < T0)
        self.hi = count_hi(SLOTS - 1) * i + count_hi(k, first, whole) - T0
        self.on_vector = k in LO_ON_VECTOR and not self.whole
        self.stacked = k == STACKED
        self.lo = (count_lo(SLOTS - 1, self.on_vector) * i + count_lo(k, self.on_vector, first, whole)
                   - count_lo(T0 - 1, self.on_vector))


class FirstSlot(Slot):

    def __init__(self, k):
        self.k, self.layer1, self.pair, self.tile = k, False, 0, k
        self.acc = 1
        self.before, self.done = k, k + 1
        self.ring = k % RING
        self.by_tensor = self.on_vector = False
        self.whole = True
        self.stacked = k == STACKED


def cin_kernel(nc, x, x_wrapped, x_cols, w0_straight, w0_mirrored, b0, w1, b1, w2, b2, sel, ident, pick_b, out):
    n_cols = x.shape[1]
    pairs = n_cols // PAIR
    last = pairs - 1
    q_cols = n_cols // 4
    samples = n_cols // D

    with ExitStack() as ctx:
        def sb(name, shape, dt=F32):
            return ctx.enter_context(nc.sbuf_tensor(name, shape, dt))

        def psum(name, shape):
            return ctx.enter_context(nc.psum_tensor(name, shape, F32))

        def sem(name):
            return ctx.enter_context(nc.semaphore(name))

        w0a = sb("w0a", [P, T0, P])
        w0b = sb("w0b", [P, T0, P])
        w1s = sb("w1s", [P, T1, P])
        w0_hi = sb("w0_hi", [P, T0, P], F32R)
        w0_lo = sb("w0_lo", [P, STACKED, P], F32R)
        w1_hi = sb("w1_hi", [P, T1, P], F32R)
        w1_lo = sb("w1_lo", [P, T1, P], F32R)
        w2s = sb("w2s", [P, 2 * FIELDS])
        b0s = sb("b0s", [P, 1])
        b1s = sb("b1s", [P, 1])
        b2s = sb("b2s", [P, 1])
        sels = sb("sels", [PARTS * FIELDS, len(SPREAD_TILES), P], BF16)
        idents = sb("idents", [P, P])
        pick_bs = sb("pick_bs", [P, 4])
        xq = sb("xq", [P, Q])
        xq_parts = sb("xq_parts", [P, PARTS, Q], BF16)
        x_rest = sb("x_rest", [PARTS * FIELDS, PAIR])
        xp = sb("xp", [PARTS * FIELDS, PAIR], BF16)
        x4_first = sb("x4_first", [P, PAIR])
        x4 = sb("x4", [P, PAIR])
        xs = sb("xs", [P, XS_RING, PAIR])
        x_shifted = sb("x_shifted", [P, T0, PAIR])
        xt = sb("xt", [P, n_cols // P * FIELDS])
        prod = sb("prod", [P, RING, PAIR])
        hi = sb("hi", [P, RING, PAIR], F32R)
        lo = sb("lo", [P, RING, PAIR], F32R)
        h1 = sb("h1", [P, PAIR])
        h2 = sb("h2", [P, CHUNK])
        direct = sb("direct", [P, PAIR])
        sums = sb("sums", [P, samples + B_PAIR])
        v = sb("v", [P, BLOCKS * FIELDS])
        z2_in = sb("z2_in", [P, BLOCKS * pairs])
        z2 = sb("z2", [P, BLOCKS * pairs])
        res = sb("res", [P, 4, P + 1])
        xe = psum("xe", [P, PAIR])
        h1_psum = psum("h1_psum", [P, PAIR])
        acc0 = psum("acc0", [P, 2, CHUNK])
        acc1 = psum("acc1", [P, 2, CHUNK])

        parts_dram = nc.dram_tensor("parts_scratch", (P, PARTS, q_cols), BF16, kind="Internal").ap()

        stacked_zeroed = sem("stacked_zeroed")
        w0_loaded = sem("w0_loaded")
        w1_loaded = [sem(f"w1_loaded{half}") for half in range(2)]
        small_loaded = sem("small_loaded")
        b0_loaded = sem("b0_loaded")
        sel_loaded = sem("sel_loaded")
        final_loaded = sem("final_loaded")
        w0_summed = sem("w0_summed")
        w_hi_ready = sem("w_hi_ready")
        w_lo_ready = sem("w_lo_ready")
        first_part_ready = sem("first_part_ready")
        first_rest_ready = sem("first_rest_ready")
        xq_loaded = sem("xq_loaded")
        part_ready = sem("part_ready")
        rest_ready = sem("rest_ready")
        parts_stored = sem("parts_stored")
        xp_loaded = sem("xp_loaded")
        x4_first_loaded = sem("x4_first_loaded")
        x4_loaded = sem("x4_loaded")
        x_shifted_loaded = [sem(f"x_shifted_loaded{t}") for t in range(T0)]
        xt_loaded = sem("xt_loaded")
        xs_loaded = [sem(f"xs_loaded{place}") for place in range(XS_RING)]
        x4_copied = sem("x4_copied")
        xe_ready = sem("xe_ready")
        h1_psum_ready = sem("h1_psum_ready")
        prod_ready = sem("prod_ready")
        hi_ready = sem("hi_ready")
        lo_vector_ready = sem("lo_vector_ready")
        lo_pool_ready = sem("lo_pool_ready")
        slot_done = sem("slot_done")
        h1_ready = sem("h1_ready")
        direct0_ready = sem("direct0_ready")
        direct1_ready = sem("direct1_ready")
        h2_ready = sem("h2_ready")
        direct_summed = sem("direct_summed")
        u_ready = sem("u_ready")
        v_ready = sem("v_ready")
        z2_summed = sem("z2_summed")
        z2_ready = sem("z2_ready")
        turned = sem("turned")
        z2_final = sem("z2_final")
        res_ready = sem("res_ready")
        stored = sem("stored")

        block = ctx.enter_context(nc.Block())

        x_q = x.rearrange("m (q j i) -> j m q i", j=4, i=Q)
        parts_q = parts_dram.rearrange("(j m) r n -> r m j n", j=4)
        x4_source = bass.AP(x.tensor, 0, [[0, 4], [n_cols, FIELDS], [1, n_cols]])
        shifted_source = [bass.AP(x_wrapped.tensor, 4 * t * n_cols, [[n_cols, 4], [n_cols, FIELDS], [1, n_cols]])
                          for t in range(STACKED)]

        @block.sync
        def _(sp):
            def load_xq(q):
                sp.dma_start(xq[:, :], x_q[:, :, bass.ds(q, 1), :]).then_inc(xq_loaded, 16)

            def load_parts(q):
                sp.wait_ge(parts_stored, 16 * q)
                for r in range(PARTS):
                    sp.dma_start(xp[r * FIELDS:(r + 1) * FIELDS, :].rearrange("p (j i) -> p j i", i=Q),
                                 parts_q[r][:, :, bass.ds(q * Q, Q)]).then_inc(xp_loaded, 16)

            def load_spread(q, n):
                source = bass.AP(x.tensor, 2 * DMA_TILES[n] * n_cols, [[n_cols, 2], [0, HALF], [1, n_cols]])
                sp.dma_start(xs[:, n % XS_RING, :], source[:, :, bass.ds(q * PAIR, PAIR)]).then_inc(xs_loaded[n % XS_RING], 16)

            def load_xt(q):
                cols = bass.ds(q * (BLOCKS * FIELDS), BLOCKS * FIELDS)
                sp.dma_start(xt[:, cols], x_cols[:, cols]).then_inc(xt_loaded, 16)

            def load_x4(q):
                sp.dma_start(x4[:, :], x4_source[:, :, bass.ds(q * PAIR, PAIR)]).then_inc(x4_loaded, 16)

            def load_shifted(t, q):
                cols = bass.ds(q * PAIR, PAIR)
                if t < STACKED:
                    sp.dma_start(x_shifted[:, t, :], shifted_source[t][:, :, cols]).then_inc(x_shifted_loaded[t], 16)
                    return
                for start in range(0, 3 * FIELDS, FIELDS):
                    sp.dma_start(x_shifted[start:start + FIELDS // 2, STACKED, :],
                                 x[FIELDS // 2:, cols]).then_inc(x_shifted_loaded[STACKED], 16)

            def body(i, is_first=False, loads_after=True, is_last=False):
                for n, tile in enumerate(DMA_TILES):
                    slot = Slot(i, T0 + tile, is_last)
                    sp.wait_ge(prod_ready, slot.done)
                    if n + XS_RING < len(DMA_TILES):
                        load_spread(i, n + XS_RING)
                    elif not is_last:
                        load_spread(i + 1, n + XS_RING - len(DMA_TILES))
                    if loads_after:
                        if n == 0:
                            if not is_first:
                                sp.wait_ge(x4_copied, i)
                            load_x4(i + 2)
                        elif n <= T0:
                            load_shifted(n - 1, i + 2)
                        elif n == T0 + 1:
                            sp.wait_ge(part_ready, PARTS * (i + 1))
                            load_xq(i + 2)
                    if n == T0 + 2:
                        load_xt(i)
                    if tile > SPREAD_TILES[-1] > DMA_TILES[n - 1] and not is_last:
                        load_parts(i + 1)

            sp.dma_start(x4_first[:, :], x4_source[:, :, 0:PAIR]).then_inc(x4_first_loaded, 16)
            for t in range(T0):
                if t == STACKED:
                    sp.wait_ge(stacked_zeroed, 1)
                load_shifted(t, 0)
            load_x4(1)
            sp.dma_start(b1s[:, :], b1).then_inc(small_loaded, 16)
            sp.dma_start(w2s[:, :], w2).then_inc(small_loaded, 16)
            sp.dma_start(b2s[:, :], b2).then_inc(small_loaded, 16)
            for t in range(T0):
                sp.wait_ge(prod_ready, t + 1)
                load_shifted(t, 1)
                if t == STACKED:
                    sp.dma_start(w1s[:, T1 // 2:, :], w1[:, T1 // 2:, :]).then_inc(w1_loaded[1], 16)
            for n in range(XS_RING):
                load_spread(0, n)
            load_xq(1)
            sp.dma_start(idents[:, :], ident).then_inc(final_loaded, 16)
            sp.dma_start(pick_bs[:, :], pick_b).then_inc(final_loaded, 16)
            body(0, is_first=True)
            with sp.Fori(1, last - 1) as i:
                body(i)
            body(last - 1, loads_after=False)
            body(last, loads_after=False, is_last=True)
            sp.wait_ge(res_ready, 3)
            sp.dma_start(out.rearrange("(q r) c -> q r c", r=4), res[:, :, :]).then_inc(stored, 16)
            sp.wait_ge(stored, 16)

        @block.tensor
        def _(pe):
            def spread(slot):
                if slot.tile == SPREAD_TILES[0]:
                    if isinstance(slot.pair, int) and slot.pair == 0:
                        pe.wait_ge(first_part_ready, 4)
                    else:
                        pe.wait_ge(xp_loaded, 16 * PARTS * slot.pair)
                if slot.spread_free is not None:
                    pe.wait_ge(prod_ready, slot.spread_free)
                for c in range(2):
                    cols = slice(c * CHUNK, (c + 1) * CHUNK)
                    mm = pe.matmul(xe[:, cols], sels[:, SPREAD_TILES.index(slot.tile), :], xp[:, cols], start=True, stop=True)
                mm.then_inc(xe_ready, 1)

            def contract(slot, c):
                acc = (acc0, acc1)[slot.acc]
                w_hi, w_lo, tiles = (w1_hi, w1_lo, T1) if slot.layer1 else (w0_hi, w0_lo, T0)
                cols = slice(c * CHUNK, (c + 1) * CHUNK)
                first, final = slot.tile == 0, slot.tile == tiles - 1
                if slot.whole:
                    if c == 0:
                        pe.wait_ge(prod_ready, slot.done)
                    weights = w1s if slot.layer1 else w0a
                    rows = slice(0, FIELDS if slot.stacked else P)
                    mm = pe.matmul(acc[:, c, :], weights[rows, slot.tile, :], prod[rows, slot.ring, cols],
                                   start=first, stop=final)
                    if c == 1:
                        mm.then_inc(slot_done, 1)
                    return
                if c == 0:
                    pe.wait_ge(hi_ready, slot.hi)
                    if slot.stacked:
                        pe.wait_ge(lo_vector_ready if slot.on_vector else lo_pool_ready, slot.lo)
                if slot.stacked:
                    mm = pe.matmul(acc[:, c, :], w_hi[:, slot.tile, :], hi[:, slot.ring, cols], start=False, stop=True)
                    if c == 1:
                        mm.then_inc(slot_done, 1)
                    return
                pe.matmul(acc[:, c, :], w_hi[:, slot.tile, :], hi[:, slot.ring, cols], start=first, stop=False)
                pe.matmul(acc[:, c, :], w_lo[:, slot.tile, :], hi[:, slot.ring, cols], start=False, stop=False)
                if c == 0:
                    pe.wait_ge(lo_vector_ready if slot.on_vector else lo_pool_ready, slot.lo)
                mm = pe.matmul(acc[:, c, :], w_hi[:, slot.tile, :], lo[:, slot.ring, cols], start=False, stop=final)
                if c == 1:
                    mm.then_inc(slot_done, 1)

            def layer2(i, free):
                pe.wait_ge(prod_ready, free)
                pe.wait_ge(h2_ready, 2 * (i + 1))
                for a in range(BLOCKS // 2):
                    mm = pe.matmul(xe[:, 2 * a * FIELDS:2 * (a + 1) * FIELDS], h2[:, a * P:(a + 1) * P], w2s[:, :],
                                   start=True, stop=True)
                mm.then_inc(u_ready, 1)

            def turn(half, summed):
                pe.wait_ge(direct_summed, summed)
                acc = (acc1, acc0)[half]
                rows = slice(half * HALF, (half + 1) * HALF)
                for r in range(4):
                    start = half * B_PAIR + r
                    mm = pe.transpose(acc[:, 0, r * HALF:(r + 1) * HALF],
                                      sums[rows, start:start + samples - 3:4], idents[rows, rows])
                mm.then_inc(turned, 1)

            def body(i, is_first=False, is_last=False, before_last=False):
                first_k = T0 if is_last else 0
                slots = [Slot(i, k, is_last) for k in range(first_k, SLOTS)]
                after = [] if is_last else [Slot(i + 1, k, before_last) for k in range(T0 if before_last else 0, SLOTS)]
                ahead = slots[AHEAD:] + after[:AHEAD]
                for n, slot in enumerate(slots):
                    if slot.k == (T0 if is_first or is_last else 0):
                        pe.wait_ge(h1_ready, 2 * (i + 1))
                        pe.wait_ge(direct0_ready, i + 1)
                    if is_first and slot.layer1 and slot.tile % (T1 // 2) == 0:
                        half = slot.tile // (T1 // 2)
                        pe.wait_ge(w_hi_ready, 2 + half)
                        pe.wait_ge(w_lo_ready, 3 + half)
                    if slot.k == T0 and not (is_first or is_last):
                        pe.wait_ge(direct1_ready, i)
                        pe.wait_ge(h2_ready, 2 * i)
                    if is_last and slot.k == SLOTS - 1:
                        turn(0, pairs)
                    if slot.k == U_AT and not is_first:
                        layer2(i - 1, Slot(i, T0 + SPREAD_TILES[-1], is_last).done)
                    if n < len(ahead) and ahead[n].by_tensor:
                        if before_last and n > U_AT:
                            pe.wait_ge(v_ready, i)
                        spread(ahead[n])
                    for c in range(2):
                        contract(slot, c)

            pe.wait_ge(w0_summed, 1)
            opening = [FirstSlot(k) for k in range(T0)]
            for slot in opening:
                for c in range(2):
                    contract(slot, c)
            pe.wait_ge(sel_loaded, 16)
            body(0, is_first=True)
            with pe.Fori(1, last - 1) as i:
                body(i)
            body(last - 1, before_last=True)
            pe.wait_ge(final_loaded, 32)
            body(last, is_last=True)
            layer2(last, T0 + SLOTS * last + T1)
            pe.wait_ge(z2_ready, 1)
            pe.matmul(xe[:, CHUNK:CHUNK + 4], z2[:, :], pick_bs[:, :], start=True, stop=True).then_inc(z2_final, 1)
            turn(1, pairs + 1)

        @block.vector
        def _(dve):
            def take_off(step, q):
                dve.wait_ge(part_ready, PARTS * (q - 1) + step + 1)
                dve.tensor_tensor(xq[:, :], xq[:, :], xq_parts[:, step, :], ALU.subtract).then_inc(rest_ready, 1)

            def multiply(slot):
                if not isinstance(slot.done, int) or slot.done > RING:
                    dve.wait_ge(slot_done, slot.done - RING)
                if slot.by_tensor:
                    if slot.tile == SPREAD_TILES[0]:
                        dve.wait_ge(h1_ready, 2 * (slot.pair + 1))
                    dve.wait_ge(xe_ready, slot.spreads)
                    dve.tensor_tensor(prod[:, slot.ring, :], xe[:, :], h1[:, :], ALU.mult).then_inc(prod_ready, 1)
                elif slot.layer1:
                    if slot.tile == DMA_TILES[0]:
                        dve.wait_ge(h1_psum_ready, 2 * (slot.pair + 1))
                    dve.wait_ge(xs_loaded[slot.dma_place], 16 * slot.dma_loads)
                    dve.tensor_tensor(prod[:, slot.ring, :], xs[:, slot.dma_place, :], h1_psum[:, :],
                                      ALU.mult).then_inc(prod_ready, 1)
                else:
                    dve.wait_ge(x_shifted_loaded[slot.tile], 16 * (3 if slot.stacked else 1) * (slot.pair + 1))
                    fields = xe
                    if isinstance(slot.pair, int) and slot.pair < 2:
                        fields = (x4_first, x4)[slot.pair]
                    elif slot.tile == 0:
                        dve.wait_ge(x4_copied, slot.pair - 1)
                    dve.tensor_tensor(prod[:, slot.ring, :], x_shifted[:, slot.tile, :], fields[:, :],
                                      ALU.mult).then_inc(prod_ready, 1)

            def make_lo(slot):
                dve.wait_ge(hi_ready, slot.hi)
                rows = slice(2 * FIELDS, 3 * FIELDS) if slot.stacked else slice(0, P)
                to = hi if slot.stacked else lo
                dve.tensor_tensor(to[rows, slot.ring, :], prod[rows, slot.ring, :], hi[rows, slot.ring, :].bitcast(F32),
                                  ALU.subtract).then_inc(lo_vector_ready, 1)

            def slots_of(slots, after):
                for n, slot in enumerate(slots):
                    multiply(slot)
                    if n >= LO_LAG and slots[n - LO_LAG].on_vector:
                        make_lo(slots[n - LO_LAG])
                    after(slot)
                for slot in slots[-LO_LAG:]:
                    if slot.on_vector:
                        make_lo(slot)

            def sum_direct(i, rows):
                dve.tensor_reduce(sums[rows, bass.ds(i * B_PAIR, B_PAIR)],
                                  direct[rows, :].rearrange("p (b d) -> p b d", d=D), AX_X, ALU.add).then_inc(direct_summed, 1)

            def use_u(i):
                dve.wait_ge(xt_loaded, 16 * (i + 1))
                dve.wait_ge(u_ready, i + 1)
                dve.tensor_tensor(v[:, :], xe[:, 0:BLOCKS * FIELDS],
                                  xt[:, bass.ds(i * (BLOCKS * FIELDS), BLOCKS * FIELDS)], ALU.mult).then_inc(v_ready, 1)

            def sum_fields(i):
                dve.wait_ge(v_ready, i + 1)
                dve.tensor_reduce(z2_in[:, bass.ds(i * BLOCKS, BLOCKS)].rearrange("p (c a) -> p a c", c=2),
                                  v[:, :].rearrange("p (a c m) -> p a c m", c=2, m=FIELDS), AX_X, ALU.add).then_inc(z2_summed, 1)

            def w1_lo_half(half):
                tiles = slice(half * T1 // 2, (half + 1) * T1 // 2)
                dve.wait_ge(w_hi_ready, 2 + half)
                dve.tensor_tensor(w1_lo[:, tiles, :], w1s[:, tiles, :], w1_hi[:, tiles, :].bitcast(F32),
                                  ALU.subtract).then_inc(w_lo_ready, 1)

            def body(i, is_first=False, is_last=False):
                def after(slot):
                    if is_first and slot.k in W1_LO_AT:
                        w1_lo_half(W1_LO_AT[slot.k])
                    if not is_last and slot.k in REST_AT:
                        take_off(REST_AT[slot.k], i + 1)
                    if slot.k == SUM_AT:
                        dve.wait_ge(direct0_ready, i + 1)
                        if not is_first:
                            dve.wait_ge(direct1_ready, i)
                        sum_direct(i, slice(0, HALF) if is_first else slice(0, P))
                    if slot.k == V_AT and not is_first:
                        use_u(i - 1)
                    if slot.k == V_SUM_AT and not is_first:
                        sum_fields(i - 1)

                if is_first:
                    dve.wait_ge(x4_loaded, 16)
                slots_of([Slot(i, k, is_last) for k in range(T0 if is_last else 0, SLOTS)], after)

            def after_first(slot):
                if slot.k == 0:
                    dve.wait_ge(w0_loaded, 32)
                    dve.tensor_tensor(w0a[:, :, :], w0a[:, :, :], w0b[:, :, :], ALU.add).then_inc(w0_summed, 1)
                if slot.k == 1:
                    dve.wait_ge(first_part_ready, 1)
                    dve.tensor_tensor(x_rest[:, :], x4_first[0:PARTS * FIELDS, :], xp[:, :], ALU.subtract).then_inc(first_rest_ready, 1)
                if slot.k == 3:
                    third = slice(2 * FIELDS, 3 * FIELDS)
                    dve.wait_ge(first_part_ready, 2)
                    dve.tensor_tensor(x_rest[third, :], x_rest[third, :], xp[third, :], ALU.subtract).then_inc(first_rest_ready, 1)
                if slot.k == 2:
                    dve.wait_ge(w_hi_ready, 1)
                    dve.tensor_tensor(w0_lo[:, :, :], w0a[:, 0:STACKED, :], w0_hi[:, 0:STACKED, :].bitcast(F32),
                                      ALU.subtract).then_inc(w_lo_ready, 1)
                    mid = slice(FIELDS, 2 * FIELDS)
                    dve.tensor_tensor(w0_hi[mid, STACKED, :], w0a[mid, STACKED, :], w0_hi[mid, STACKED, :].bitcast(F32),
                                      ALU.subtract).then_inc(w_lo_ready, 1)

            dve.wait_ge(x4_first_loaded, 16)
            slots_of([FirstSlot(k) for k in range(T0)], after_first)
            body(0, is_first=True)
            with dve.Fori(1, last) as i:
                body(i)
            body(last, is_last=True)
            dve.wait_ge(slot_done, T0 + SLOTS * last + T1)
            dve.tensor_scalar(h2[HALF:P, :], acc0[0:HALF, 1, :], b1s[0:HALF, :], 0.0, ALU.add, ALU.max).then_inc(h2_ready, 1)
            use_u(last)
            sum_fields(last)
            dve.wait_ge(direct1_ready, pairs)
            sum_direct(pairs, slice(HALF, P))
            dve.wait_ge(turned, 2)
            dve.tensor_copy(res[:, :, HALF:P], acc0[:, 0, 0:4 * HALF].rearrange("p (r a) -> p r a", a=HALF)).then_inc(res_ready, 1)

        @block.gpsimd
        def _(pool):
            def slots_of(slots):
                for slot in slots:
                    if not (slot.on_vector or slot.whole):
                        pool.wait_ge(hi_ready, slot.hi)
                        pool.tensor_tensor(lo[:, slot.ring, :], prod[:, slot.ring, :], hi[:, slot.ring, :].bitcast(F32),
                                           ALU.subtract).then_inc(lo_pool_ready, 1)

            pool.memset(x_shifted[:, STACKED, :], 0.0).then_inc(stacked_zeroed, 1)
            slots_of([Slot(0, k) for k in range(SLOTS)])
            with pool.Fori(1, last) as i:
                slots_of([Slot(i, k) for k in range(SLOTS)])
            slots_of([Slot(last, k, True) for k in range(T0, SLOTS)])

        @block.scalar
        def _(act):
            act.dma_start(w0a[:, :, :], w0_straight).then_inc(w0_loaded, 16)
            act.dma_start(w0b[:, :, :], w0_mirrored).then_inc(w0_loaded, 16)
            act.dma_start(b0s[:, :], b0).then_inc(b0_loaded, 16)

            def part(step, q):
                if step:
                    act.wait_ge(rest_ready, 2 * (q - 1) + step)
                else:
                    act.wait_ge(xq_loaded, 16 * q)
                    if not isinstance(q, int) or q > 1:
                        act.wait_ge(parts_stored, 16 * (q - 1))
                act.activation(xq_parts[:, step, :], xq[:, :], ACT.Copy).then_inc(part_ready, 1)

            def store_parts(q):
                act.wait_ge(part_ready, PARTS * q)
                act.dma_start(parts_dram[:, :, bass.ds(q * Q, Q)], xq_parts[:, :, :]).then_inc(parts_stored, 16)

            def make_hi(slot):
                if slot.whole:
                    return
                act.wait_ge(prod_ready, slot.done)
                act.activation(hi[:, slot.ring, :], prod[:, slot.ring, :], ACT.Copy).then_inc(hi_ready, 1)

            def leave_hidden0(i, step, is_first=False):
                acc = acc1 if is_first else acc0
                if step == 0 and is_first:
                    act.wait_ge(slot_done, T0)
                if step == 0 and not is_first:
                    act.wait_ge(prod_ready, T0 + SLOTS * i)
                to, ready = (h1_psum, h1_psum_ready) if step < 2 else (h1, h1_ready)
                half = step % 2
                act.activation(to[half * HALF:(half + 1) * HALF, :], acc[0:HALF, :, :].rearrange("p c n -> p (c n)"),
                               ACT.Relu, bias=b0s[0:HALF, :]).then_inc(ready, 1)

            def leave_direct0(i, done, acc=acc0):
                act.wait_ge(slot_done, done)
                if not isinstance(i, int) or i > 0:
                    act.wait_ge(direct_summed, i)
                act.activation(direct[0:HALF, :], acc[HALF:P, :, :].rearrange("p c n -> p (c n)"), ACT.Relu,
                               bias=b0s[HALF:P, :]).then_inc(direct0_ready, 1)

            def leave_hidden1(i, done, acc=acc1, chunks=(0, 1)):
                act.wait_ge(slot_done, done)
                for c in chunks:
                    act.activation(h2[c * HALF:(c + 1) * HALF, :], acc[0:HALF, c, :], ACT.Relu,
                                   bias=b1s[0:HALF, :]).then_inc(h2_ready, 1)

            def leave_direct1(i, acc=acc1):
                act.wait_ge(direct_summed, i + 1)
                act.activation(direct[HALF:P, :], acc[HALF:P, :, :].rearrange("p c n -> p (c n)"), ACT.Relu,
                               bias=b1s[HALF:P, :]).then_inc(direct1_ready, 1)

            def copy_x4(q, is_first=False):
                act.wait_ge(prod_ready, Slot(q - 2, T0 + SPREAD_TILES[-1]).done)
                if not is_first:
                    act.wait_ge(v_ready, q - 2)
                act.wait_ge(x4_loaded, 16 * q)
                act.activation(xe[:, :], x4[:, :], ACT.Copy).then_inc(x4_copied, 1)

            def w1_hi_half(half):
                tiles = slice(half * T1 // 2, (half + 1) * T1 // 2)
                act.wait_ge(w1_loaded[half], 16)
                act.activation(w1_hi[:, tiles, :], w1s[:, tiles, :], ACT.Copy).then_inc(w_hi_ready, 1)

            def body(i, is_first=False, is_last=False, has_after=True):
                first_k = T0 if is_last else 0
                if is_last:
                    for step in range(4):
                        leave_hidden0(i, step)
                for slot in [Slot(i, k, is_last) for k in range(first_k, SLOTS)]:
                    make_hi(slot)
                    if is_first and slot.k == W1_HI_AT:
                        w1_hi_half(1)
                    if not is_last and slot.k in HIDDEN0_AT:
                        for step in HIDDEN0_AT[slot.k]:
                            leave_hidden0(i, step, is_first)
                    if is_first and slot.k == 4:
                        leave_direct0(0, T0, acc1)
                    if not is_first and slot.k == (T0 if is_last else LAYER1_AT):
                        leave_hidden1(i - 1, T0 + SLOTS * i)
                    if not is_first and slot.k == (T0 + 1 if is_last else LAYER1_AT):
                        leave_direct1(i - 1)
                    if not is_last:
                        if slot.k in ROUND_AT:
                            part(ROUND_AT[slot.k], i + 1)
                            if ROUND_AT[slot.k] == PARTS - 1:
                                store_parts(i + 1)
                        if has_after and slot.k == X4_AT:
                            copy_x4(i + 2, is_first)
                        if slot.k == DIRECT0_AT:
                            leave_direct0(i + 1, T0 + SLOTS * i + T0)

            second, third = slice(FIELDS, 2 * FIELDS), slice(2 * FIELDS, PARTS * FIELDS)
            act.wait_ge(x4_first_loaded, 16)
            act.activation(xp[:, :], x4_first[0:PARTS * FIELDS, :], ACT.Copy).then_inc(first_part_ready, 1)
            act.wait_ge(w0_summed, 1)
            act.activation(w0_hi[:, :, :], w0a[:, :, :], ACT.Copy).then_inc(w_hi_ready, 1)
            act.dma_start(w1s[:, :T1 // 2, :], w1[:, :T1 // 2, :]).then_inc(w1_loaded[0], 16)
            act.dma_start(sels[:, :, :], sel).then_inc(sel_loaded, 16)
            act.wait_ge(first_rest_ready, 1)
            act.activation(xp[third, :], x_rest[third, :], ACT.Copy).then_inc(first_part_ready, 1)
            act.activation(xp[second, :], x_rest[second, :], ACT.Copy).then_inc(first_part_ready, 1)
            act.wait_ge(first_rest_ready, 2)
            act.activation(xp[third, :], x_rest[third, :], ACT.Copy).then_inc(first_part_ready, 1)
            w1_hi_half(0)
            act.wait_ge(b0_loaded, 16)
            body(0, is_first=True)
            act.wait_ge(small_loaded, 16 * 3)
            with act.Fori(1, last - 1) as i:
                body(i)
            body(last - 1, has_after=False)
            body(last, is_last=True)
            act.wait_ge(turned, 1)
            act.activation(res[:, :, 0:HALF], acc1[:, 0, 0:4 * HALF].rearrange("p (r a) -> p r a", a=HALF),
                           ACT.Copy).then_inc(res_ready, 1)
            leave_hidden1(last, T0 + SLOTS * last + T1, acc0, (0,))
            leave_direct1(last, acc0)
            act.wait_ge(z2_summed, pairs)
            act.activation(z2[:, :], z2_in[:, :], ACT.Relu, bias=b2s[:, :]).then_inc(z2_ready, 1)
            act.wait_ge(z2_final, 1)
            act.activation(res[:, :, P:P + 1], xe[:, CHUNK:CHUNK + 4].rearrange("p (r a) -> p r a", a=1),
                           ACT.Copy).then_inc(res_ready, 1)


def kernel(r_x, L0_rec_W0, L0_rec_b0, L0_rec_W1, L0_rec_b1, L0_rec_W2, L0_rec_b2):
    import numpy as np
    import ml_dtypes
    import concourse.bacc as bacc
    from concourse.bass_utils import run_bass_kernel_spmd

    samples, fields, d = r_x.shape
    x = np.ascontiguousarray(np.asarray(r_x).transpose(1, 0, 2)).reshape(fields, samples * d)
    x_cols = np.ascontiguousarray(x.reshape(fields, -1, 2, BLOCKS // 2, P).transpose(4, 1, 3, 2, 0)).reshape(P, -1)
    w0 = np.asarray(L0_rec_W0).reshape(P, fields, fields)
    straight = np.zeros((P, T0, P), w0.dtype)
    mirrored = np.zeros((P, T0, P), w0.dtype)
    for s in range(17):
        m = np.arange(fields if s < 16 else fields // 2)
        for copy in range(3 if s == 16 else 1):
            rows = (s % 4 + copy) * fields + m
            straight[rows, s // 4] = w0[:, m, (m + s) % fields].T
            if s:
                mirrored[rows, s // 4] = w0[:, (m + s) % fields, m].T
    w1 = np.asarray(L0_rec_W1).reshape(P, HALF, T1, 2).transpose(3, 1, 2, 0)
    w1 = np.ascontiguousarray(w1).reshape(P, T1, P)

    w2 = np.zeros((2, HALF, 2, fields), np.asarray(L0_rec_W2).dtype)
    for chunk in range(2):
        w2[chunk, :, chunk] = np.asarray(L0_rec_W2).reshape(HALF, fields)
    sel = np.zeros((PARTS, fields, len(SPREAD_TILES), P), np.float32)
    for n, t in enumerate(SPREAD_TILES):
        for half in range(2):
            sel[:, 2 * t + half, n, half * HALF:(half + 1) * HALF] = 1
    sel = sel.reshape(PARTS * fields, -1, P).astype(ml_dtypes.bfloat16)
    ident = np.eye(P, dtype=np.float32)
    pick_b = np.repeat(np.eye(4, dtype=np.float32), d, axis=0)

    arrays = {
        "x": x, "x_wrapped": np.concatenate([x, x[:fields // 2]]), "x_cols": x_cols, "w0_straight": straight, "w0_mirrored": mirrored,
        "b0": np.asarray(L0_rec_b0).reshape(P, 1), "w1": w1, "b1": np.asarray(L0_rec_b1).reshape(P, 1),
        "w2": w2.reshape(P, 2 * fields), "b2": np.ascontiguousarray(np.broadcast_to(np.asarray(L0_rec_b2).reshape(1, 1), (P, 1))),
        "sel": sel, "ident": ident, "pick_b": pick_b,
    }
    nc = bacc.Bacc("TRN2", target_bir_lowering=False, num_devices=1)
    ins = {n: nc.dram_tensor(f"in_{n}", v.shape, mybir.dt.from_np(v.dtype), kind="ExternalInput").ap()
           for n, v in arrays.items()}
    out = nc.dram_tensor("out_0", (samples, P + 1), F32, kind="ExternalOutput").ap()
    cin_kernel(nc, *ins.values(), out)
    r = run_bass_kernel_spmd(nc, [{f"in_{n}": v for n, v in arrays.items()}], core_ids=[0])
    return r.results[0]["out_0"]
```
